# Optimizing a Trainium2 kernel written in Bass

```python
import numpy as np
import jax
import jax.numpy as jnp

def _softmax(x, axis=-1):
    return jax.nn.softmax(x, axis=axis)

def _gelu(x):
    return jax.nn.gelu(x, approximate=True)

def _silu(x):
    return jax.nn.silu(x)

def _sigmoid(x):
    return jax.nn.sigmoid(x)

def _layernorm(x, axis=-1, eps=1e-05):
    m = jnp.mean(x, axis=axis, keepdims=True)
    v = jnp.var(x, axis=axis, keepdims=True)
    return (x - m) / jnp.sqrt(v + eps)

def _scatter_add(tgt, idx, src, axis=0):
    return tgt.at[idx].add(src)

def _segment_sum(src, seg, n):
    return jax.ops.segment_sum(src, seg, n)
kernel_name = 'mk_dlrm_tower_d1_rec_r8_6d516f'

def setup_inputs(seed: int=0):
    np.random.seed(seed)
    _w = jnp.asarray

    def _rec_inputs():
        import jax
        import jax.numpy as jnp
        _tk = jax.random.key(seed)
        dense_ctx = jax.random.normal(jax.random.fold_in(_tk, 190), (1024, 16), jnp.float32)
        ids = jnp.stack([jax.random.randint(jax.random.fold_in(_tk, 200 + f), (1024,), 0, v, jnp.int32) for f, v in enumerate([125000, 1000, 1250, 12500, 1250, 1000, 1000, 12500, 12500, 1250, 1000, 12500, 1000, 1250, 12500, 1250, 1000, 12500, 1250, 1000, 12500, 12500, 1000, 1250, 1250, 1000, 1000, 1000, 1250, 1250, 1250, 1000, 1250, 1000, 1250, 1000, 1000, 1000, 1000, 1000])], axis=1)
        tbl_0 = 0.05 * jax.random.normal(jax.random.fold_in(_tk, 500 + 0), (125000, 128), jnp.float32)
        tbl_1 = 0.05 * jax.random.normal(jax.random.fold_in(_tk, 500 + 1), (1000, 128), jnp.float32)
        tbl_2 = 0.05 * jax.random.normal(jax.random.fold_in(_tk, 500 + 2), (1250, 128), jnp.float32)
        tbl_3 = 0.05 * jax.random.normal(jax.random.fold_in(_tk, 500 + 3), (12500, 128), jnp.float32)
        tbl_4 = 0.05 * jax.random.normal(jax.random.fold_in(_tk, 500 + 4), (1250, 128), jnp.float32)
        tbl_5 = 0.05 * jax.random.normal(jax.random.fold_in(_tk, 500 + 5), (1000, 128), jnp.float32)
        tbl_6 = 0.05 * jax.random.normal(jax.random.fold_in(_tk, 500 + 6), (1000, 128), jnp.float32)
        tbl_7 = 0.05 * jax.random.normal(jax.random.fold_in(_tk, 500 + 7), (12500, 128), jnp.float32)
        tbl_8 = 0.05 * jax.random.normal(jax.random.fold_in(_tk, 500 + 8), (12500, 128), jnp.float32)
        tbl_9 = 0.05 * jax.random.normal(jax.random.fold_in(_tk, 500 + 9), (1250, 128), jnp.float32)
        tbl_10 = 0.05 * jax.random.normal(jax.random.fold_in(_tk, 500 + 10), (1000, 128), jnp.float32)
        tbl_11 = 0.05 * jax.random.normal(jax.random.fold_in(_tk, 500 + 11), (12500, 128), jnp.float32)
        tbl_12 = 0.05 * jax.random.normal(jax.random.fold_in(_tk, 500 + 12), (1000, 128), jnp.float32)
        tbl_13 = 0.05 * jax.random.normal(jax.random.fold_in(_tk, 500 + 13), (1250, 128), jnp.float32)
        tbl_14 = 0.05 * jax.random.normal(jax.random.fold_in(_tk, 500 + 14), (12500, 128), jnp.float32)
        tbl_15 = 0.05 * jax.random.normal(jax.random.fold_in(_tk, 500 + 15), (1250, 128), jnp.float32)
        tbl_16 = 0.05 * jax.random.normal(jax.random.fold_in(_tk, 500 + 16), (1000, 128), jnp.float32)
        tbl_17 = 0.05 * jax.random.normal(jax.random.fold_in(_tk, 500 + 17), (12500, 128), jnp.float32)
        tbl_18 = 0.05 * jax.random.normal(jax.random.fold_in(_tk, 500 + 18), (1250, 128), jnp.float32)
        tbl_19 = 0.05 * jax.random.normal(jax.random.fold_in(_tk, 500 + 19), (1000, 128), jnp.float32)
        tbl_20 = 0.05 * jax.random.normal(jax.random.fold_in(_tk, 500 + 20), (12500, 128), jnp.float32)
        tbl_21 = 0.05 * jax.random.normal(jax.random.fold_in(_tk, 500 + 21), (12500, 128), jnp.float32)
        tbl_22 = 0.05 * jax.random.normal(jax.random.fold_in(_tk, 500 + 22), (1000, 128), jnp.float32)
        tbl_23 = 0.05 * jax.random.normal(jax.random.fold_in(_tk, 500 + 23), (1250, 128), jnp.float32)
        tbl_24 = 0.05 * jax.random.normal(jax.random.fold_in(_tk, 500 + 24), (1250, 128), jnp.float32)
        tbl_25 = 0.05 * jax.random.normal(jax.random.fold_in(_tk, 500 + 25), (1000, 128), jnp.float32)
        tbl_26 = 0.05 * jax.random.normal(jax.random.fold_in(_tk, 500 + 26), (1000, 128), jnp.float32)
        tbl_27 = 0.05 * jax.random.normal(jax.random.fold_in(_tk, 500 + 27), (1000, 128), jnp.float32)
        tbl_28 = 0.05 * jax.random.normal(jax.random.fold_in(_tk, 500 + 28), (1250, 128), jnp.float32)
        tbl_29 = 0.05 * jax.random.normal(jax.random.fold_in(_tk, 500 + 29), (1250, 128), jnp.float32)
        tbl_30 = 0.05 * jax.random.normal(jax.random.fold_in(_tk, 500 + 30), (1250, 128), jnp.float32)
        tbl_31 = 0.05 * jax.random.normal(jax.random.fold_in(_tk, 500 + 31), (1000, 128), jnp.float32)
        tbl_32 = 0.05 * jax.random.normal(jax.random.fold_in(_tk, 500 + 32), (1250, 128), jnp.float32)
        tbl_33 = 0.05 * jax.random.normal(jax.random.fold_in(_tk, 500 + 33), (1000, 128), jnp.float32)
        tbl_34 = 0.05 * jax.random.normal(jax.random.fold_in(_tk, 500 + 34), (1250, 128), jnp.float32)
        tbl_35 = 0.05 * jax.random.normal(jax.random.fold_in(_tk, 500 + 35), (1000, 128), jnp.float32)
        tbl_36 = 0.05 * jax.random.normal(jax.random.fold_in(_tk, 500 + 36), (1000, 128), jnp.float32)
        tbl_37 = 0.05 * jax.random.normal(jax.random.fold_in(_tk, 500 + 37), (1000, 128), jnp.float32)
        tbl_38 = 0.05 * jax.random.normal(jax.random.fold_in(_tk, 500 + 38), (1000, 128), jnp.float32)
        tbl_39 = 0.05 * jax.random.normal(jax.random.fold_in(_tk, 500 + 39), (1000, 128), jnp.float32)
        _rk = jax.random.fold_in(_tk, 7)
        W_top1 = 0.0354441 * jax.random.normal(jax.random.fold_in(_tk, 801), (796, 512), jnp.float32)
        W_top2 = 0.0441942 * jax.random.normal(jax.random.fold_in(_tk, 802), (512, 256), jnp.float32)
        W_top3 = 0.0625 * jax.random.normal(jax.random.fold_in(_tk, 803), (256, 1), jnp.float32)
        b_top1 = jnp.zeros((512,), jnp.float32)
        b_top2 = jnp.zeros((256,), jnp.float32)
        return (dense_ctx, ids, tbl_0, tbl_1, tbl_2, tbl_3, tbl_4, tbl_5, tbl_6, tbl_7, tbl_8, tbl_9, tbl_10, tbl_11, tbl_12, tbl_13, tbl_14, tbl_15, tbl_16, tbl_17, tbl_18, tbl_19, tbl_20, tbl_21, tbl_22, tbl_23, tbl_24, tbl_25, tbl_26, tbl_27, tbl_28, tbl_29, tbl_30, tbl_31, tbl_32, tbl_33, tbl_34, tbl_35, tbl_36, tbl_37, tbl_38, tbl_39, W_top1, b_top1, W_top2, b_top2, W_top3)
    dense_ctx, ids, tbl_0, tbl_1, tbl_2, tbl_3, tbl_4, tbl_5, tbl_6, tbl_7, tbl_8, tbl_9, tbl_10, tbl_11, tbl_12, tbl_13, tbl_14, tbl_15, tbl_16, tbl_17, tbl_18, tbl_19, tbl_20, tbl_21, tbl_22, tbl_23, tbl_24, tbl_25, tbl_26, tbl_27, tbl_28, tbl_29, tbl_30, tbl_31, tbl_32, tbl_33, tbl_34, tbl_35, tbl_36, tbl_37, tbl_38, tbl_39, W_top1, b_top1, W_top2, b_top2, W_top3 = _rec_inputs()

    def _L0_rec_setup():
        import jax, jax.numpy as jnp
        import numpy as np
        NUM_FIELDS = 40
        EMBED_DIM = 128
        BATCH = 1024
        NUM_IX = NUM_FIELDS * (NUM_FIELDS - 1) // 2

        def _pair_indices(num_fields):
            row, col = ([], [])
            for i in range(num_fields - 1):
                for j in range(i + 1, num_fields):
                    row.append(i)
                    col.append(j)
            return (np.asarray(row, dtype=np.int32), np.asarray(col, dtype=np.int32))
        key = jax.random.key(seed)
        k1, k2 = jax.random.split(key)
        x = jax.random.normal(k1, (BATCH, NUM_FIELDS, EMBED_DIM), dtype=jnp.float32)
        kernel = jax.random.normal(k2, (EMBED_DIM, NUM_IX, EMBED_DIM), dtype=jnp.float32) * 0.05
        return {'x': x, 'kernel': kernel}
    _L0_rec_all = _L0_rec_setup()
    _L0_rec_in = {k: v for k, v in _L0_rec_all.items() if k in ('kernel',)}
    del _L0_rec_all
    return {'dense_ctx': dense_ctx, 'ids': ids, 'tbl_0': tbl_0, 'tbl_1': tbl_1, 'tbl_2': tbl_2, 'tbl_3': tbl_3, 'tbl_4': tbl_4, 'tbl_5': tbl_5, 'tbl_6': tbl_6, 'tbl_7': tbl_7, 'tbl_8': tbl_8, 'tbl_9': tbl_9, 'tbl_10': tbl_10, 'tbl_11': tbl_11, 'tbl_12': tbl_12, 'tbl_13': tbl_13, 'tbl_14': tbl_14, 'tbl_15': tbl_15, 'tbl_16': tbl_16, 'tbl_17': tbl_17, 'tbl_18': tbl_18, 'tbl_19': tbl_19, 'tbl_20': tbl_20, 'tbl_21': tbl_21, 'tbl_22': tbl_22, 'tbl_23': tbl_23, 'tbl_24': tbl_24, 'tbl_25': tbl_25, 'tbl_26': tbl_26, 'tbl_27': tbl_27, 'tbl_28': tbl_28, 'tbl_29': tbl_29, 'tbl_30': tbl_30, 'tbl_31': tbl_31, 'tbl_32': tbl_32, 'tbl_33': tbl_33, 'tbl_34': tbl_34, 'tbl_35': tbl_35, 'tbl_36': tbl_36, 'tbl_37': tbl_37, 'tbl_38': tbl_38, 'tbl_39': tbl_39, 'W_top1': W_top1, 'b_top1': b_top1, 'W_top2': W_top2, 'b_top2': b_top2, 'W_top3': W_top3, 'L0_rec_kernel': _L0_rec_in['kernel']}

def reference(dense_ctx, ids, tbl_0, tbl_1, tbl_2, tbl_3, tbl_4, tbl_5, tbl_6, tbl_7, tbl_8, tbl_9, tbl_10, tbl_11, tbl_12, tbl_13, tbl_14, tbl_15, tbl_16, tbl_17, tbl_18, tbl_19, tbl_20, tbl_21, tbl_22, tbl_23, tbl_24, tbl_25, tbl_26, tbl_27, tbl_28, tbl_29, tbl_30, tbl_31, tbl_32, tbl_33, tbl_34, tbl_35, tbl_36, tbl_37, tbl_38, tbl_39, W_top1, b_top1, W_top2, b_top2, W_top3, L0_rec_kernel):
    import jax
    import jax.numpy as jnp

    def _L0_rec_ref(x, kernel):
        import jax, jax.numpy as jnp
        import numpy as np
        NUM_FIELDS = 40
        EMBED_DIM = 128
        BATCH = 1024
        NUM_IX = NUM_FIELDS * (NUM_FIELDS - 1) // 2

        def _pair_indices(num_fields):
            row, col = ([], [])
            for i in range(num_fields - 1):
                for j in range(i + 1, num_fields):
                    row.append(i)
                    col.append(j)
            return (np.asarray(row, dtype=np.int32), np.asarray(col, dtype=np.int32))
        row, col = _pair_indices(x.shape[1])
        p = x[:, row, :]
        q = x[:, col, :]
        kp = jnp.einsum('bnd,end,bne->bn', p, kernel, q)
        return kp
    e = jnp.stack([tbl_0[ids[:, 0]], tbl_1[ids[:, 1]], tbl_2[ids[:, 2]], tbl_3[ids[:, 3]], tbl_4[ids[:, 4]], tbl_5[ids[:, 5]], tbl_6[ids[:, 6]], tbl_7[ids[:, 7]], tbl_8[ids[:, 8]], tbl_9[ids[:, 9]], tbl_10[ids[:, 10]], tbl_11[ids[:, 11]], tbl_12[ids[:, 12]], tbl_13[ids[:, 13]], tbl_14[ids[:, 14]], tbl_15[ids[:, 15]], tbl_16[ids[:, 16]], tbl_17[ids[:, 17]], tbl_18[ids[:, 18]], tbl_19[ids[:, 19]], tbl_20[ids[:, 20]], tbl_21[ids[:, 21]], tbl_22[ids[:, 22]], tbl_23[ids[:, 23]], tbl_24[ids[:, 24]], tbl_25[ids[:, 25]], tbl_26[ids[:, 26]], tbl_27[ids[:, 27]], tbl_28[ids[:, 28]], tbl_29[ids[:, 29]], tbl_30[ids[:, 30]], tbl_31[ids[:, 31]], tbl_32[ids[:, 32]], tbl_33[ids[:, 33]], tbl_34[ids[:, 34]], tbl_35[ids[:, 35]], tbl_36[ids[:, 36]], tbl_37[ids[:, 37]], tbl_38[ids[:, 38]], tbl_39[ids[:, 39]]], axis=1)
    z = _L0_rec_ref(e, L0_rec_kernel)
    z = z.reshape(z.shape[0], -1)
    h = jnp.concatenate([z, dense_ctx], axis=1)
    h = jnp.maximum(h @ W_top1 + b_top1, 0.0)
    h = jnp.maximum(h @ W_top2 + b_top2, 0.0)
    y = h @ W_top3
    return y

_drawn_inputs = setup_inputs


def setup_inputs(seed=0):
    import zlib

    import numpy as np

    out = dict(_drawn_inputs(seed))
    spreads = {'b_top1': (0.0, 0.1), 'b_top2': (0.0, 0.1)}
    factors = {'tbl_0': 3.239,
     'tbl_1': 2.873,
     'tbl_2': 3.042,
     'tbl_3': 2.867,
     'tbl_4': 2.969,
     'tbl_5': 2.703,
     'tbl_6': 3.181,
     'tbl_7': 2.917,
     'tbl_8': 2.721,
     'tbl_10': 2.891,
     'tbl_11': 2.995,
     'tbl_13': 2.802,
     'tbl_14': 2.879,
     'tbl_15': 3.044,
     'tbl_16': 2.962,
     'tbl_17': 2.762,
     'tbl_18': 3.326,
     'tbl_19': 2.981,
     'tbl_20': 2.676,
     'tbl_21': 3.07,
     'tbl_22': 2.939,
     'tbl_23': 2.7,
     'tbl_24': 3.171,
     'tbl_25': 3.043,
     'tbl_26': 2.706,
     'tbl_27': 2.946,
     'tbl_28': 2.864,
     'tbl_29': 2.901,
     'tbl_30': 2.908,
     'tbl_32': 3.023,
     'tbl_33': 2.903,
     'tbl_34': 3.048,
     'tbl_35': 2.718,
     'tbl_36': 3.122,
     'tbl_37': 3.117,
     'tbl_38': 2.946,
     'tbl_39': 2.727}
    for name, (base, spread) in spreads.items():
        noise = np.random.default_rng([zlib.crc32(name.encode()), seed]).standard_normal(out[name].shape)
        drawn = base * np.exp(spread * noise) if base else spread * noise
        out[name] = jnp.asarray(drawn.astype(out[name].dtype))
    for name, factor in factors.items():
        out[name] = (out[name] * factor).astype(out[name].dtype)
    return out
```

```python
from contextlib import ExitStack

import numpy as np

import concourse.bass as bass
from concourse import mybir

F32 = mybir.dt.float32
F32R = mybir.dt.float32r
I32 = mybir.dt.int32
U32 = mybir.dt.uint32
ALU = mybir.AluOpType
ACT = mybir.ActivationFunctionType
AX = mybir.AxisListType

PART = 128
FIELDS = 40
EMBED = 128
BATCH = 1024
DENSE = 16
PAIRS = FIELDS * (FIELDS - 1) // 2
IN1, OUT1, OUT2 = PAIRS + DENSE, 512, 256
BT = BATCH // PART
GROUP = 4
COLS = GROUP * EMBED
TILES = BT // 2
RAW, SPLIT = 3, 3
ZS = 3
AHEAD = 2
LEAD = 3
UNITS = sum(-(-j // GROUP) for j in range(1, FIELDS))
SCRATCH = 8192


def row_start(j):
    return j * (j - 1) // 2


def first_unit(j):
    return sum(-(-f // GROUP) for f in range(1, j))


def unit_pairs(u):
    j = next(f for f in range(1, FIELDS) if first_unit(f + 1) > u)
    return j % GROUP if j % GROUP and u == first_unit(j) else GROUP


def reducer(j, t):
    return ("pool", "act", "act" if j % GROUP == 0 else "dve", "act")[t]


def tower(nc, dense_ctx, ids, tables, kernels, W1, b1, W2, b2, W3, y, z_dram):
    ctx = ExitStack()
    with ctx:
        def sb(name, shape, dt=F32):
            return ctx.enter_context(nc.sbuf_tensor(name, shape, dt))

        def sem(name):
            return ctx.enter_context(nc.semaphore(name))

        x = sb("x", [PART, BT, FIELDS, EMBED])
        xT = sb("xT", [PART, 2, 2, BATCH], F32R)
        k_raw = sb("k_raw", [PART, RAW * COLS])
        k_high = sb("k_high", [PART, SPLIT * COLS], F32R)
        k_low = sb("k_low", [PART, SPLIT * COLS], F32R)
        prod = sb("prod", [PART, TILES, 2, COLS])
        z = sb("z", [PART, ZS, BT, FIELDS])
        idx = sb("idx", [PART, BT, FIELDS], I32)
        ident = sb("ident", [PART, PART])
        psum = ctx.enter_context(nc.psum_tensor("psum", [PART, TILES, 2, COLS], F32))

        ids_loaded = sem("ids_loaded")
        gathered = [sem(f"gathered{r}") for r in range(GROUP)]
        ident_ready = sem("ident_ready")
        k_loaded = sem("k_loaded")
        k_high_ready = sem("k_high_ready")
        k_low_ready = sem("k_low_ready")
        xT_in_psum = sem("xT_in_psum")
        xT_high_ready = sem("xT_high_ready")
        xT_low_ready = sem("xT_low_ready")
        dots_ready = sem("dots_ready")
        mult_done = sem("mult_done")
        folded = sem("folded")
        summed = [sem(f"summed{t}") for t in range(TILES)]
        z_stored = [sem(f"z_stored{s}") for s in range(ZS)]
        h_loaded = sem("h_loaded")
        w1_loaded = sem("w1_loaded")
        w_loaded = sem("w_loaded")
        hT_in_psum = sem("hT_in_psum")
        hT_ready = [sem(f"hT_ready{e}") for e in ("_act", "_dve")]
        l1_in_psum = sem("l1_in_psum")
        l1_ready = sem("l1_ready")
        l2_in_psum = sem("l2_in_psum")
        l2_ready = sem("l2_ready")
        y_in_psum = sem("y_in_psum")
        y_ready = sem("y_ready")
        y_stored = sem("y_stored")

        FOLDS = 3

        flat = x[:, :, :, :].rearrange("p t f d -> p (t f d)")
        CH = -(-IN1 // PART)
        chunk_rows = [min(PART, IN1 - PART * c) for c in range(CH)]
        at = [0]

        def carve(n):
            at[0] += n
            return flat[:, at[0] - n:at[0]]

        h = carve(BT * IN1).rearrange("p (t n) -> p t n", t=BT)
        hT = carve(CH * BATCH).rearrange("p (c b) -> p c b", c=CH)
        w1 = carve(CH * OUT1).rearrange("p (c n) -> p c n", c=CH)
        C1, C2 = OUT1 // PART, OUT2 // PART
        l1T = carve(C1 * BATCH).rearrange("p (c b) -> p c b", c=C1)
        w2 = carve(C1 * OUT2).rearrange("p (c n) -> p c n", c=C1)
        l2T = carve(C2 * BATCH).rearrange("p (c b) -> p c b", c=C2)
        w3 = carve(C2)
        bias1 = carve(C1)
        bias2 = carve(C2)
        y_row = carve(BATCH)
        HALF = BATCH // 2

        def units(eng, j, body, stop=None):
            short, full, u0 = j % GROUP, j // GROUP, first_unit(j)
            if short:
                body(u0, full * GROUP, short, True)
                u0 += 1
            if full:
                with eng.Fori(0, full) as g:
                    body(u0 + g, g * GROUP, GROUP, False)

        def held(eng, value):
            return value if isinstance(value, int) else eng.compute_val(value)

        def raw_slot(u):
            return (u % RAW) * COLS

        def split_slot(u):
            return (u % SPLIT) * COLS

        block = ctx.enter_context(nc.Block())

        @block.sync
        def _(sp):
            sp.dma_start(idx[:, :, :], ids.rearrange("(t p) f -> p t f", p=PART)).then_inc(ids_loaded, 16)

            def load(u, i0, pairs, j):
                cols = pairs * EMBED if j < GROUP else COLS
                pair0 = row_start(j) + i0 + pairs - cols // EMBED
                to, source = held(sp, raw_slot(u) + COLS - cols), held(sp, pair0 * EMBED)
                earlier, freed = held(sp, u * 16), held(sp, u - RAW + 1)
                if j > 1:
                    sp.wait_ge(k_loaded, earlier)
                if j >= GROUP:
                    sp.wait_ge(k_low_ready, freed)
                sp.dma_start(k_raw[:, bass.ds(to, cols)], kernels[:, bass.ds(source, cols)]).then_inc(k_loaded, 16)

            for j in range(1, FIELDS):
                units(sp, j, lambda u, i0, pairs, first: load(u, i0, pairs, j))

            sp.wait_ge(mult_done, UNITS * TILES)
            full = IN1 // PART
            sp.dma_start(w1[:, 0:full, :], W1[0:full * PART, :].rearrange("(c p) n -> p c n", p=PART)).then_inc(w1_loaded, 16)
            sp.dma_start(w1[0:chunk_rows[-1], full, :], W1[full * PART:IN1, :]).then_inc(w1_loaded, 16)
            for s in range(ZS):
                sp.wait_ge(z_stored[s], 16 * len(range(s or ZS, FIELDS, ZS)))
            sp.dma_start(h[:, :, 0:PAIRS], z_dram.rearrange("(t p) n -> p t n", p=PART)).then_inc(h_loaded, 16)
            sp.dma_start(h[:, :, PAIRS:IN1], dense_ctx.rearrange("(t p) n -> p t n", p=PART)).then_inc(h_loaded, 16)
            sp.dma_start(w2, W2.rearrange("(c p) n -> p c n", p=PART)).then_inc(w_loaded, 16)
            with nc.allow_non_contiguous_dma(reason="vectors of at most 512 elements, one per partition"):
                sp.dma_start(w3, W3.rearrange("(c p) n -> p (c n)", p=PART)).then_inc(w_loaded, 16)
                sp.dma_start(bias1, b1.rearrange("(c p) -> p c", p=PART)).then_inc(w_loaded, 16)
                sp.dma_start(bias2, b2.rearrange("(c p) -> p c", p=PART)).then_inc(w_loaded, 16)
            sp.wait_ge(y_ready, 2)
            sp.dma_start(y.rearrange("b n -> n b"), y_row[0:1, :]).then_inc(y_stored, 16)
            sp.wait_ge(y_stored, 16)

        @block.gpsimd
        def _(pool):
            nc.gpsimd.memset(ident[:, :], 0.0).then_inc(ident_ready, 1)
            pool.wait_ge(ident_ready, 1)
            nc.gpsimd.affine_select(out=ident[:, :], in_=ident[:, :], compare_op=ALU.not_equal, fill=1.0,
                                    base=0, pattern=[[-1, PART]], channel_multiplier=1).then_inc(ident_ready, 1)
            pool.wait_ge(ids_loaded, 16)

            def gather(f):
                if f >= GROUP:
                    pool.wait_ge(gathered[f % GROUP], 16 * BT * (f // GROUP))
                for t in range(BT):
                    nc.gpsimd.indirect_dma_start(
                        x[:, t, f, :], None, tables[f],
                        bass.IndirectOffsetOnAxis(ap=idx[:, t, f:f + 1].bitcast(U32), axis=0)
                    ).then_inc(gathered[f % GROUP], 16)

            def split_low(u, pairs=GROUP):
                skip = COLS - pairs * EMBED
                raw, part = held(pool, raw_slot(u) + skip), held(pool, split_slot(u) + skip)
                pool.wait_ge(k_high_ready, u + 1)
                if not isinstance(u, int) or u >= SPLIT:
                    pool.wait_ge(dots_ready, TILES * (u - SPLIT + 1))
                nc.gpsimd.tensor_tensor(
                    k_low[:, bass.ds(part, COLS - skip)], k_raw[:, bass.ds(raw, COLS - skip)],
                    k_high[:, bass.ds(part, COLS - skip)].bitcast(F32), ALU.subtract).then_inc(k_low_ready, 1)

            def unit(u, i0, pairs, first):
                if not isinstance(u, int):
                    split_low(u + AHEAD)
                elif u + AHEAD < UNITS:
                    split_low(u + AHEAD, unit_pairs(u + AHEAD) if u + AHEAD < RAW else GROUP)
                pool.wait_ge(mult_done, TILES * u + 1)
                p = prod[:, 0, :, 0:pairs * EMBED].rearrange("p b (n d) -> p b n d", d=EMBED)
                for s in range(FOLDS):
                    w = EMBED >> (s + 1)
                    if s:
                        pool.wait_ge(folded, FOLDS * u + s)
                    nc.gpsimd.tensor_tensor(p[:, :, :, 0:w], p[:, :, :, 0:w], p[:, :, :, w:2 * w],
                                            ALU.add).then_inc(folded, 1)

            for f in range(2):
                gather(f)
            for u in range(AHEAD):
                split_low(u, unit_pairs(u))
            for f in range(2, LEAD + 1):
                gather(f)
            for j in range(1, FIELDS):
                if j + LEAD < FIELDS:
                    gather(j + LEAD)
                if j < FIELDS - 1:
                    units(pool, j, unit)
                else:
                    u0 = first_unit(j)
                    unit(u0, j // GROUP * GROUP, j % GROUP, True)
                    with pool.Fori(0, j // GROUP - AHEAD) as g:
                        unit(u0 + 1 + g, g * GROUP, GROUP, False)
                    for g in range(j // GROUP - AHEAD, j // GROUP):
                        unit(u0 + 1 + g, g * GROUP, GROUP, False)

        @block.scalar
        def _(act):
            def split_high(u, pairs=GROUP):
                skip = COLS - pairs * EMBED
                raw, part = held(act, raw_slot(u) + skip), held(act, split_slot(u) + skip)
                act.wait_ge(k_loaded, 16 * (u + 1))
                if not isinstance(u, int) or u >= SPLIT:
                    act.wait_ge(dots_ready, TILES * (u - SPLIT + 1))
                    act.wait_ge(k_low_ready, u - SPLIT + 1)
                nc.scalar.activation(k_high[:, bass.ds(part, COLS - skip)], k_raw[:, bass.ds(raw, COLS - skip)], ACT.Copy).then_inc(k_high_ready, 1)

            def split_x_high(j):
                act.wait_ge(xT_in_psum, j)
                nc.scalar.activation(xT[:, j % 2, 0, :], psum[:, TILES - 1, :, :].rearrange("p a b -> p (a b)"),
                                     ACT.Copy).then_inc(xT_high_ready, 1)

            def store(j):
                for t in range(TILES):
                    act.wait_ge(summed[t], first_unit(j + 1))
                zj = z_dram[:, row_start(j):row_start(j) + j].rearrange("(t p) n -> p t n", p=PART)
                with nc.allow_non_contiguous_dma(reason="field 1 has one pair"):
                    act.dma_start(zj, z[:, j % ZS, :, 0:j]).then_inc(z_stored[j % ZS], 16)

            def field(j):

                def unit(u, i0, pairs, first):
                    if not isinstance(u, int):
                        split_high(u + AHEAD)
                    elif u + AHEAD < UNITS:
                        split_high(u + AHEAD, unit_pairs(u + AHEAD) if u + AHEAD < RAW else GROUP)
                    if first and j + 1 < FIELDS:
                        split_x_high(j + 1)
                    for t in range(TILES):
                        if reducer(j, t) != "act":
                            continue
                        act.wait_ge(mult_done, TILES * u + t + 1)
                        for b in range(2):
                            for n in range(pairs):
                                p = prod[:, t, b, n * EMBED:(n + 1) * EMBED]
                                last = nc.scalar.activation(p, p, ACT.Copy,
                                                            accum_out=z[:, j % ZS, 2 * t + b, bass.ds(i0 + n, 1)])
                        last.then_inc(summed[t], 1)

                if j > ZS:
                    act.wait_ge(z_stored[j % ZS], 16 * ((j - 1) // ZS))
                if j % GROUP == 0:
                    split_x_high(j + 1)
                if j < FIELDS - 1:
                    units(act, j, unit)
                else:
                    u0 = first_unit(j)
                    unit(u0, j // GROUP * GROUP, j % GROUP, True)
                    with act.Fori(0, j // GROUP - AHEAD) as g:
                        unit(u0 + 1 + g, g * GROUP, GROUP, False)
                    for g in range(j // GROUP - AHEAD, j // GROUP):
                        unit(u0 + 1 + g, g * GROUP, GROUP, False)

            for u in range(AHEAD):
                split_high(u, unit_pairs(u))
            split_x_high(1)
            for j in range(1, FIELDS):
                field(j)
                if j > 1:
                    store(j - 1)
            store(FIELDS - 1)

            for c in range(0, CH, 2):
                act.wait_ge(hT_in_psum, c + 1)
                nc.scalar.activation(hT[0:chunk_rows[c], c, :], psum[0:chunk_rows[c], c % TILES, :, :].rearrange("p a b -> p (a b)"),
                                     ACT.Copy).then_inc(hT_ready[0], 1)
            act.wait_ge(w_loaded, 64)
            for c in range(C1):
                for half in range(2):
                    act.wait_ge(l1_in_psum, 2 * c + half + 1)
                    nc.scalar.activation(l1T[:, c, half * HALF:(half + 1) * HALF], psum[:, c, half, :], ACT.Relu,
                                         bias=bias1[:, c:c + 1]).then_inc(l1_ready, 1)
            for c in range(C2):
                for half in range(2):
                    act.wait_ge(l2_in_psum, 2 * c + half + 1)
                    nc.scalar.activation(l2T[:, c, half * HALF:(half + 1) * HALF], psum[:, c, half, :], ACT.Relu,
                                         bias=bias2[:, c:c + 1]).then_inc(l2_ready, 1)
            for half in range(2):
                act.wait_ge(y_in_psum, half + 1)
                nc.scalar.activation(y_row[0:1, half * HALF:(half + 1) * HALF], psum[0:1, C2, half, :], ACT.Copy).then_inc(y_ready, 1)

        @block.vector
        def _(dve):
            def split_x_low(j):
                dve.wait_ge(xT_high_ready, j)
                nc.vector.tensor_tensor(xT[:, j % 2, 1, :], psum[:, TILES - 1, :, :].rearrange("p a b -> p (a b)"),
                                        xT[:, j % 2, 0, :].bitcast(F32), ALU.subtract).then_inc(xT_low_ready, 1)

            def field(j):
                def unit(u, i0, pairs, first):
                    cols = pairs * EMBED
                    i0 = held(dve, i0)
                    for t in range(TILES):
                        if t == TILES - 1 and first and j + 1 < FIELDS:
                            split_x_low(j + 1)
                        dve.wait_ge(dots_ready, TILES * u + t + 1)
                        if not (isinstance(u, int) and u == 0):
                            dve.wait_ge(summed[t], u)
                        nc.vector.tensor_tensor(
                            prod[:, t, :, 0:cols], psum[:, t, :, 0:cols],
                            x[:, 2 * t:2 * t + 2, bass.ds(i0, pairs), :].rearrange("p b n d -> p b (n d)"),
                            ALU.mult).then_inc(mult_done, 1)
                    for t in reversed(range(TILES)):
                        who = reducer(j, t)
                        if who == "act":
                            continue
                        width = EMBED
                        if who == "pool":
                            dve.wait_ge(folded, FOLDS * (u + 1))
                            width = EMBED >> FOLDS
                        else:
                            dve.wait_ge(mult_done, TILES * u + t + 1)
                        p = prod[:, t, :, 0:cols].rearrange("p b (n d) -> p b n d", d=EMBED)
                        nc.vector.tensor_reduce(z[:, j % ZS, 2 * t:2 * t + 2, bass.ds(i0, pairs)], p[:, :, :, 0:width],
                                                AX.X, ALU.add).then_inc(summed[t], 1)

                if j > ZS:
                    dve.wait_ge(z_stored[j % ZS], 16 * ((j - 1) // ZS))
                if j % GROUP == 0:
                    split_x_low(j + 1)
                units(dve, j, unit)

            split_x_low(1)
            dve.wait_ge(gathered[0], 16 * BT)
            for j in range(1, FIELDS):
                field(j)

            for c in range(1, CH, 2):
                dve.wait_ge(hT_in_psum, c + 1)
                nc.vector.tensor_copy(hT[0:chunk_rows[c], c, :], psum[0:chunk_rows[c], c % TILES, :, :].rearrange("p a b -> p (a b)")
                                      ).then_inc(hT_ready[1], 1)

        @block.tensor
        def _(pe):
            def transpose_x(j):
                pe.wait_ge(gathered[j % GROUP], 16 * BT * (j // GROUP + 1))
                if j > 2 or j == 2:
                    if first_unit(j - 1) > 0:
                        pe.wait_ge(mult_done, TILES * first_unit(j - 1))
                    pe.wait_ge(xT_low_ready, j - 1)
                for t in range(BT):
                    last = nc.tensor.transpose(psum[:, TILES - 1, t // 4, (t % 4) * PART:(t % 4 + 1) * PART],
                                               x[:, t, j, :], ident[:, :])
                last.then_inc(xT_in_psum, 1)

            def field(j):
                par = j % 2

                def unit(u, i0, pairs, first):
                    cols = pairs * EMBED
                    part = held(pe, split_slot(u) + COLS - cols)
                    high, low = k_high[:, bass.ds(part, cols)], k_low[:, bass.ds(part, cols)]
                    pe.wait_ge(k_low_ready, u + 1)
                    for t in range(TILES):
                        if t == 2 and first and j + 1 < FIELDS:
                            transpose_x(j + 1)
                        if not (isinstance(u, int) and u == 0):
                            pe.wait_ge(mult_done, TILES * (u - 1) + t + 1)
                        if t == TILES - 1 and j + 1 < FIELDS:
                            pe.wait_ge(xT_low_ready, j + 1)
                        for b in range(2):
                            out = psum[:, t, b, 0:cols]
                            bt = 2 * t + b
                            x_high = xT[:, par, 0, bt * PART:(bt + 1) * PART]
                            x_low = xT[:, par, 1, bt * PART:(bt + 1) * PART]
                            nc.tensor.matmul(out, x_high, high, start=True, stop=False)
                            nc.tensor.matmul(out, x_high, low, start=False, stop=False)
                            last = nc.tensor.matmul(out, x_low, high, start=False, stop=True)
                        last.then_inc(dots_ready, 1)

                pe.wait_ge(xT_low_ready, j)
                if j % GROUP == 0:
                    transpose_x(j + 1)
                units(pe, j, unit)

            pe.wait_ge(ident_ready, 2)
            transpose_x(1)
            for j in range(1, FIELDS):
                field(j)

            pe.wait_ge(h_loaded, 32)
            pe.wait_ge(mult_done, UNITS * TILES)
            for c in range(CH):
                if c >= TILES:
                    pe.wait_ge(hT_ready[c % 2], (c - TILES) // 2 + 1)
                for t in range(BT):
                    last = nc.tensor.transpose(psum[0:chunk_rows[c], c % TILES, t // 4, (t % 4) * PART:(t % 4 + 1) * PART],
                                               h[:, t, c * PART:c * PART + chunk_rows[c]], ident[:, :])
                last.then_inc(hT_in_psum, 1)
            pe.wait_ge(w1_loaded, 32)
            pe.wait_ge(hT_ready[0], -(-CH // 2))
            pe.wait_ge(hT_ready[1], CH // 2)
            for c in range(C1):
                for half in range(2):
                    for k in range(CH):
                        rows = chunk_rows[k]
                        last = nc.tensor.matmul(psum[:, c, half, :], w1[0:rows, k, c * PART:(c + 1) * PART],
                                                hT[0:rows, k, half * HALF:(half + 1) * HALF], start=k == 0, stop=k == CH - 1)
                    last.then_inc(l1_in_psum, 1)
            pe.wait_ge(w_loaded, 64)
            pe.wait_ge(l1_ready, 2 * C1)
            for c in range(C2):
                for half in range(2):
                    for k in range(C1):
                        last = nc.tensor.matmul(psum[:, c, half, :], w2[:, k, c * PART:(c + 1) * PART],
                                                l1T[:, k, half * HALF:(half + 1) * HALF], start=k == 0, stop=k == C1 - 1)
                    last.then_inc(l2_in_psum, 1)
            pe.wait_ge(l2_ready, 2 * C2)
            for half in range(2):
                for k in range(C2):
                    last = nc.tensor.matmul(psum[0:1, C2, half, :], w3[:, k:k + 1],
                                            l2T[:, k, half * HALF:(half + 1) * HALF], start=k == 0, stop=k == C2 - 1)
                last.then_inc(y_in_psum, 1)


def kernel(**inputs):
    import concourse.bacc as bacc
    from concourse.bass_utils import run_bass_kernel_spmd

    number = {}
    for i in range(FIELDS - 1):
        for j in range(i + 1, FIELDS):
            number[i, j] = len(number)
    order = [number[i, j] for j in range(1, FIELDS) for i in range(j)]

    nc = bacc.Bacc("TRN2", target_bir_lowering=False, num_devices=1, dynamic_dma_scratch_size=SCRATCH)
    arrays, aps = {}, {}

    def give(name, a):
        a = np.ascontiguousarray(a)
        arrays[name] = a
        aps[name] = nc.dram_tensor(name, a.shape, mybir.dt.from_np(a.dtype), kind="ExternalInput").ap()
        return aps[name]

    dense_ctx = give("dense_ctx", inputs["dense_ctx"])
    ids = give("ids", inputs["ids"])
    tables = [give(f"tbl_{f}", inputs[f"tbl_{f}"]) for f in range(FIELDS)]
    kernels = give("kernels", np.asarray(inputs["L0_rec_kernel"])[:, order, :].reshape(EMBED, PAIRS * EMBED))
    w1 = np.asarray(inputs["W_top1"])
    W1 = give("W1", np.concatenate([w1[order], w1[PAIRS:]]))
    b1 = give("b1", inputs["b_top1"])
    W2 = give("W2", inputs["W_top2"])
    b2 = give("b2", inputs["b_top2"])
    W3 = give("W3", inputs["W_top3"])
    y = nc.dram_tensor("y", (BATCH, 1), F32, kind="ExternalOutput").ap()
    z_dram = nc.dram_tensor("z_dram", (BATCH, PAIRS), F32, kind="Internal").ap()
    tower(nc, dense_ctx, ids, tables, kernels, W1, b1, W2, b2, W3, y, z_dram)
    result = run_bass_kernel_spmd(nc, [arrays], core_ids=[0])
    return result.results[0]["y"]
```

```python
from contextlib import ExitStack
from functools import cache

import numpy as np

import concourse.bass as bass
from concourse import mybir

F32 = mybir.dt.float32
F32R = mybir.dt.float32r
I32 = mybir.dt.int32
U32 = mybir.dt.uint32
ALU = mybir.AluOpType
ACT = mybir.ActivationFunctionType
AX = mybir.AxisListType

PART = 128
FIELDS = 40
EMBED = 128
BATCH = 1024
DENSE = 16
PAIRS = FIELDS * (FIELDS - 1) // 2
IN1, OUT1, OUT2 = PAIRS + DENSE, 512, 256
BT = BATCH // PART
GROUP = 4
COLS = GROUP * EMBED
TILES = BT // 2
RAW, SPLIT = 3, 3
ZS = 3
AHEAD = 2
FIRST_GATHERED = 14
LEAD = 2.3
POOL_FROM = 12
LATE_UNTIL = 8
KL_AT = 3
SUM_AT = 2
XT_AT = 1
FOLD_FROM = 12
SCRATCH = 8192


def row_start(j):
    return j * (j - 1) // 2


def heads(j):
    short = {0: [], 1: [3, 2] if j > 1 else [1], 2: [2], 3: [3]}[j % GROUP]
    return short + [GROUP] * ((j - sum(short)) // GROUP if j < LATE_UNTIL else 1)


def host(j):
    return first_unit(j) + len(heads(j)) - 1


def looped(j):
    return (j - sum(heads(j))) // GROUP


@cache
def first_unit(j):
    return sum(len(heads(f)) + looped(f) for f in range(1, j))


@cache
def unit_field(u):
    return next(f for f in range(1, FIELDS) if first_unit(f + 1) > u)


@cache
def unit_pairs(u):
    j = unit_field(u)
    return (heads(j) + [GROUP] * looped(j))[u - first_unit(j)]


def unit_partner(u):
    return sum(unit_pairs(v) for v in range(first_unit(unit_field(u)), u))


UNITS = first_unit(FIELDS)


FOLDS = 3


def reducer(u, t):
    if t % 2:
        return "act"
    return "pool" if t == 0 and folds(u) else "dve"


def folds(u):
    return unit_field(u) >= FOLD_FROM and unit_pairs(u) == GROUP


def gathers_through(u):
    j = unit_field(u)
    at = j + (u + 1 - first_unit(j)) / (first_unit(j + 1) - first_unit(j))
    return max(BT * FIRST_GATHERED, int(BT * min(FIELDS, at + LEAD)))


POOL_FIRST = first_unit(POOL_FROM) + AHEAD


@cache
def folded_before(u):
    return sum(folds(v) for v in range(u))


def fold_slot(u):
    return folded_before(u) % 2 * 2


def tower(nc, dense_ctx, ids, tables, kernels, W1, b1, W2, b2, W3, y, z_dram):
    ctx = ExitStack()
    with ctx:
        def sb(name, shape, dt=F32):
            return ctx.enter_context(nc.sbuf_tensor(name, shape, dt))

        def sem(name):
            return ctx.enter_context(nc.semaphore(name))

        x = sb("x", [PART, BT, FIELDS, EMBED])
        xT = sb("xT", [PART, 2, 2, BATCH], F32R)
        k_raw = sb("k_raw", [PART, RAW * COLS])
        k_high = sb("k_high", [PART, SPLIT * COLS], F32R)
        k_low = sb("k_low", [PART, SPLIT * COLS], F32R)
        prod = sb("prod", [PART, TILES, 2, COLS])
        z = sb("z", [PART, ZS, BT, FIELDS])
        idx = sb("idx", [PART, BT, FIELDS], I32)
        ident = sb("ident", [PART, PART])
        psum = ctx.enter_context(nc.psum_tensor("psum", [PART, TILES, 2, COLS], F32))

        ids_loaded = sem("ids_loaded")
        gathered = [sem(f"gathered{r}") for r in range(GROUP)]
        ident_ready = sem("ident_ready")
        k_loaded = sem("k_loaded")
        k_high_ready = sem("k_high_ready")
        k_low_ready = sem("k_low_ready")
        xT_in_psum = sem("xT_in_psum")
        xT_high_ready = sem("xT_high_ready")
        xT_low_ready = sem("xT_low_ready")
        dots_ready = sem("dots_ready")
        mult_done = sem("mult_done")
        folded = sem("folded")
        summed = {t: sem(f"act_summed{t}") for t in range(1, TILES, 2)}
        fold_summed = sem("fold_summed")
        z_stored = [sem(f"z_stored{s}") for s in range(ZS)]
        h_loaded = sem("h_loaded")
        w1_loaded = sem("w1_loaded")
        w_loaded = sem("w_loaded")
        hT_in_psum = sem("hT_in_psum")
        hT_ready = [sem(f"hT_ready{e}") for e in ("_act", "_dve")]
        l1_in_psum = sem("l1_in_psum")
        l1_ready = sem("l1_ready")
        l2_in_psum = sem("l2_in_psum")
        l2_ready = sem("l2_ready")
        y_in_psum = sem("y_in_psum")
        y_ready = sem("y_ready")
        y_stored = sem("y_stored")


        flat = x[:, :, :, :].rearrange("p t f d -> p (t f d)")
        CH = -(-IN1 // PART)
        chunk_rows = [min(PART, IN1 - PART * c) for c in range(CH)]
        at = [0]

        def carve(n):
            at[0] += n
            return flat[:, at[0] - n:at[0]]

        h = carve(BT * IN1).rearrange("p (t n) -> p t n", t=BT)
        hT = carve(CH * BATCH).rearrange("p (c b) -> p c b", c=CH)
        w1 = carve(CH * OUT1).rearrange("p (c n) -> p c n", c=CH)
        C1, C2 = OUT1 // PART, OUT2 // PART
        l1T = carve(C1 * BATCH).rearrange("p (c b) -> p c b", c=C1)
        w2 = carve(C1 * OUT2).rearrange("p (c n) -> p c n", c=C1)
        l2T = carve(C2 * BATCH).rearrange("p (c b) -> p c b", c=C2)
        w3 = carve(C2)
        bias1 = carve(C1)
        bias2 = carve(C2)
        y_row = carve(BATCH)
        HALF = BATCH // 2

        def units(eng, j, body, peel=0):
            u, i0 = first_unit(j), 0
            for pairs in heads(j):
                body(u, i0, pairs)
                u, i0 = u + 1, i0 + pairs
            if looped(j) > peel:
                with eng.Fori(0, looped(j) - peel) as g:
                    body(u + g, i0 + g * GROUP, GROUP)
            for g in range(looped(j) - peel, looped(j) if peel else 0):
                body(u + g, i0 + g * GROUP, GROUP)

        def held(eng, value):
            return value if isinstance(value, int) else eng.compute_val(value)

        def raw_slot(u):
            return (u % RAW) * COLS

        def split_slot(u):
            return (u % SPLIT) * COLS

        block = ctx.enter_context(nc.Block())

        @block.sync
        def _(sp):
            sp.dma_start(idx[:, :, :], ids.rearrange("(t p) f -> p t f", p=PART)).then_inc(ids_loaded, 16)

            def load(u, i0, pairs, j):
                cols = pairs * EMBED if j < GROUP else COLS
                pair0 = row_start(j) + i0 + pairs - cols // EMBED
                to, source = held(sp, raw_slot(u) + COLS - cols), held(sp, pair0 * EMBED)
                earlier, freed = held(sp, u * 16), held(sp, u - RAW + 1)
                if j > 1:
                    sp.wait_ge(k_loaded, earlier)
                if j >= GROUP:
                    sp.wait_ge(k_low_ready, freed)
                sp.dma_start(k_raw[:, bass.ds(to, cols)], kernels[:, bass.ds(source, cols)]).then_inc(k_loaded, 16)

            for j in range(1, FIELDS):
                units(sp, j, lambda u, i0, pairs: load(u, i0, pairs, j))

            sp.wait_ge(mult_done, UNITS * TILES)
            full = IN1 // PART
            sp.dma_start(w1[:, 0:full, :], W1[0:full * PART, :].rearrange("(c p) n -> p c n", p=PART)).then_inc(w1_loaded, 16)
            sp.dma_start(w1[0:chunk_rows[-1], full, :], W1[full * PART:IN1, :]).then_inc(w1_loaded, 16)
            for s in range(ZS):
                sp.wait_ge(z_stored[s], 16 * len(range(s or ZS, FIELDS, ZS)))
            sp.dma_start(h[:, :, 0:PAIRS], z_dram.rearrange("(t p) n -> p t n", p=PART)).then_inc(h_loaded, 16)
            sp.dma_start(h[:, :, PAIRS:IN1], dense_ctx.rearrange("(t p) n -> p t n", p=PART)).then_inc(h_loaded, 16)
            sp.dma_start(w2, W2.rearrange("(c p) n -> p c n", p=PART)).then_inc(w_loaded, 16)
            with nc.allow_non_contiguous_dma(reason="vectors of at most 512 elements, one per partition"):
                sp.dma_start(w3, W3.rearrange("(c p) n -> p (c n)", p=PART)).then_inc(w_loaded, 16)
                sp.dma_start(bias1, b1.rearrange("(c p) -> p c", p=PART)).then_inc(w_loaded, 16)
                sp.dma_start(bias2, b2.rearrange("(c p) -> p c", p=PART)).then_inc(w_loaded, 16)
            sp.wait_ge(y_ready, 2)
            sp.dma_start(y.rearrange("b n -> n b"), y_row[0:1, :]).then_inc(y_stored, 16)
            sp.wait_ge(y_stored, 16)

        @block.gpsimd
        def _(pool):
            nc.gpsimd.memset(ident[:, :], 0.0).then_inc(ident_ready, 1)
            pool.wait_ge(ident_ready, 1)
            nc.gpsimd.affine_select(out=ident[:, :], in_=ident[:, :], compare_op=ALU.not_equal, fill=1.0,
                                    base=0, pattern=[[-1, PART]], channel_multiplier=1).then_inc(ident_ready, 1)
            pool.wait_ge(ids_loaded, 16)

            def gather(n):
                f, t = divmod(n, BT)
                if f >= GROUP and t == 0:
                    pool.wait_ge(gathered[f % GROUP], 16 * BT * (f // GROUP))
                nc.gpsimd.indirect_dma_start(
                    x[:, t, f, :], None, tables[f],
                    bass.IndirectOffsetOnAxis(ap=idx[:, t, f:f + 1].bitcast(U32), axis=0)
                ).then_inc(gathered[f % GROUP], 16)

            def split_low(u):
                raw, part = raw_slot(u), split_slot(u)
                pool.wait_ge(k_high_ready, u + 1)
                pool.wait_ge(dots_ready, TILES * (u - SPLIT + 1))
                if u == POOL_FIRST:
                    pool.wait_ge(k_low_ready, u)
                nc.gpsimd.tensor_tensor(k_low[:, part:part + COLS], k_raw[:, raw:raw + COLS],
                                        k_high[:, part:part + COLS].bitcast(F32), ALU.subtract).then_inc(k_low_ready, 1)

            def fold(u):
                pool.wait_ge(mult_done, TILES * u + 1)
                p = prod[:, fold_slot(u), :, :].rearrange("p b (n d) -> p b n d", d=EMBED)
                for s in range(FOLDS):
                    w = EMBED >> (s + 1)
                    if s:
                        pool.wait_ge(folded, FOLDS * folded_before(u) + s)
                    nc.gpsimd.tensor_tensor(p[:, :, :, 0:w], p[:, :, :, 0:w], p[:, :, :, w:2 * w],
                                            ALU.add).then_inc(folded, 1)

            for f in (1, 0, *range(2, FIRST_GATHERED)):
                for t in range(BT):
                    gather(f * BT + t)
            done = FIRST_GATHERED * BT
            for u in range(UNITS):
                j = unit_field(u)
                if folds(u):
                    fold(u)
                if POOL_FIRST <= u + AHEAD < UNITS:
                    split_low(u + AHEAD)
                for n in range(done, gathers_through(u)):
                    gather(n)
                done = gathers_through(u)

        @block.scalar
        def _(act):
            def split_high(u, pairs=GROUP):
                skip = COLS - pairs * EMBED
                raw, part = held(act, raw_slot(u) + skip), held(act, split_slot(u) + skip)
                act.wait_ge(k_loaded, 16 * (u + 1))
                if not isinstance(u, int) or u >= SPLIT:
                    act.wait_ge(dots_ready, TILES * (u - SPLIT + 1))
                    act.wait_ge(k_low_ready, u - SPLIT + 1)
                nc.scalar.activation(k_high[:, bass.ds(part, COLS - skip)], k_raw[:, bass.ds(raw, COLS - skip)], ACT.Copy).then_inc(k_high_ready, 1)

            def split_x_high(j):
                act.wait_ge(xT_in_psum, j)
                nc.scalar.activation(xT[:, j % 2, 0, :], psum[:, TILES - 1, :, :].rearrange("p a b -> p (a b)"),
                                     ACT.Copy).then_inc(xT_high_ready, 1)

            def store(j):
                for t in summed:
                    act.wait_ge(summed[t], first_unit(j + 1))
                act.wait_ge(mult_done, TILES * first_unit(j + 1))
                if folded_before(first_unit(j + 1)):
                    act.wait_ge(fold_summed, folded_before(first_unit(j + 1)))
                zj = z_dram[:, row_start(j):row_start(j) + j].rearrange("(t p) n -> p t n", p=PART)
                with nc.allow_non_contiguous_dma(reason="field 1 has one pair"):
                    act.dma_start(zj, z[:, j % ZS, :, 0:j]).then_inc(z_stored[j % ZS], 16)

            def sum_tile(u, t, j, i0, pairs, between=None):
                act.wait_ge(mult_done, TILES * u + t + 1)
                for b in range(2):
                    if b and between:
                        between()
                    for n in range(pairs):
                        p = prod[:, t, b, n * EMBED:(n + 1) * EMBED]
                        last = nc.scalar.activation(p, p, ACT.Copy, accum_out=z[:, j % ZS, 2 * t + b, bass.ds(i0 + n, 1)])
                last.then_inc(summed[t], 1)

            def field(j):
                def unit(u, i0, pairs):
                    makes_x = isinstance(u, int) and u == host(j) and j + 1 < FIELDS
                    if isinstance(u, int) and u > 0:
                        before = unit_field(u - 1), unit_partner(u - 1), unit_pairs(u - 1)
                    else:
                        before = j, i0 - GROUP, GROUP
                    if isinstance(u, int) and u == 0:
                        split_x_high(2)
                    else:
                        sum_tile(u - 1, TILES - 1, *before, (lambda: split_x_high(j + 1)) if makes_x else None)
                    if not isinstance(u, int):
                        split_high(u + AHEAD)
                    elif u + AHEAD < UNITS:
                        split_high(u + AHEAD, unit_pairs(u + AHEAD) if u + AHEAD < RAW else GROUP)
                    sum_tile(u, 1, j, i0, pairs)

                if j > ZS:
                    act.wait_ge(z_stored[j % ZS], 16 * ((j - 1) // ZS))
                if j < FIELDS - 1:
                    units(act, j, unit)
                else:
                    units(act, j, unit, peel=AHEAD)

            for u in range(AHEAD):
                split_high(u, unit_pairs(u))
            split_x_high(1)
            for j in range(1, FIELDS):
                field(j)
                if j > 1:
                    store(j - 1)
            sum_tile(UNITS - 1, TILES - 1, FIELDS - 1, unit_partner(UNITS - 1), unit_pairs(UNITS - 1))
            store(FIELDS - 1)

            for c in range(0, CH, 2):
                act.wait_ge(hT_in_psum, c + 1)
                nc.scalar.activation(hT[0:chunk_rows[c], c, :], psum[0:chunk_rows[c], c % TILES, :, :].rearrange("p a b -> p (a b)"),
                                     ACT.Copy).then_inc(hT_ready[0], 1)
            act.wait_ge(w_loaded, 64)
            for c in range(C1):
                for half in range(2):
                    act.wait_ge(l1_in_psum, 2 * c + half + 1)
                    nc.scalar.activation(l1T[:, c, half * HALF:(half + 1) * HALF], psum[:, c, half, :], ACT.Relu,
                                         bias=bias1[:, c:c + 1]).then_inc(l1_ready, 1)
            for c in range(C2):
                for half in range(2):
                    act.wait_ge(l2_in_psum, 2 * c + half + 1)
                    nc.scalar.activation(l2T[:, c, half * HALF:(half + 1) * HALF], psum[:, c, half, :], ACT.Relu,
                                         bias=bias2[:, c:c + 1]).then_inc(l2_ready, 1)
            for half in range(2):
                act.wait_ge(y_in_psum, half + 1)
                nc.scalar.activation(y_row[0:1, half * HALF:(half + 1) * HALF], psum[0:1, C2, half, :], ACT.Copy).then_inc(y_ready, 1)

        @block.vector
        def _(dve):
            def split_low(u):
                cols = unit_pairs(u) * EMBED if u < RAW else COLS
                raw_end, end = raw_slot(u) + COLS, split_slot(u) + COLS
                dve.wait_ge(k_high_ready, u + 1)
                if u >= SPLIT:
                    dve.wait_ge(dots_ready, TILES * (u - SPLIT + 1))
                nc.vector.tensor_tensor(k_low[:, end - cols:end], k_raw[:, raw_end - cols:raw_end],
                                        k_high[:, end - cols:end].bitcast(F32), ALU.subtract).then_inc(k_low_ready, 1)

            def split_x_low(j):
                dve.wait_ge(xT_high_ready, j)
                nc.vector.tensor_tensor(xT[:, j % 2, 1, :], psum[:, TILES - 1, :, :].rearrange("p a b -> p (a b)"),
                                        xT[:, j % 2, 0, :].bitcast(F32), ALU.subtract).then_inc(xT_low_ready, 1)

            def sum_folded(u):
                j, i0, pairs = unit_field(u), unit_partner(u), unit_pairs(u)
                dve.wait_ge(folded, FOLDS * (folded_before(u) + 1))
                p = prod[:, fold_slot(u), :, :].rearrange("p b (n d) -> p b n d", d=EMBED)
                nc.vector.tensor_reduce(z[:, j % ZS, 0:2, i0:i0 + pairs], p[:, :, :, 0:EMBED >> FOLDS],
                                        AX.X, ALU.add).then_inc(fold_summed, 1)

            def unit(u):
                j, i0, pairs = unit_field(u), unit_partner(u), unit_pairs(u)
                cols = pairs * EMBED
                for t in range(TILES):
                    if t == KL_AT and u + AHEAD < POOL_FIRST:
                        split_low(u + AHEAD)
                    if t == XT_AT and u == host(j) and j + 1 < FIELDS:
                        split_x_low(j + 1)
                    if t == SUM_AT and u and folds(u - 1):
                        sum_folded(u - 1)
                    dve.wait_ge(dots_ready, TILES * u + t + 1)
                    if reducer(u, t) == "dve":
                        for b in range(2):
                            for n in range(pairs):
                                p = psum[:, t, b, n * EMBED:(n + 1) * EMBED]
                                last = nc.vector.scalar_tensor_tensor(
                                    p, p, 1.0, x[:, 2 * t + b, i0 + n, :], ALU.mult, ALU.mult,
                                    accum_out=z[:, j % ZS, 2 * t + b, i0 + n:i0 + n + 1])
                        last.then_inc(mult_done, 1)
                        continue
                    if reducer(u, t) == "pool":
                        slot = fold_slot(u)
                        if folded_before(u) >= 2:
                            dve.wait_ge(fold_summed, folded_before(u) - 1)
                    else:
                        slot = t
                        if u:
                            dve.wait_ge(summed[t], u)
                    nc.vector.tensor_tensor(
                        prod[:, slot, :, 0:cols], psum[:, t, :, 0:cols],
                        x[:, 2 * t:2 * t + 2, i0:i0 + pairs, :].rearrange("p b n d -> p b (n d)"),
                        ALU.mult).then_inc(mult_done, 1)

            for u in range(AHEAD):
                split_low(u)
            split_x_low(1)
            dve.wait_ge(gathered[0], 16 * BT)
            for j in range(1, FIELDS):
                if j > ZS:
                    dve.wait_ge(z_stored[j % ZS], 16 * ((j - 1) // ZS))
                for u in range(first_unit(j), first_unit(j + 1)):
                    unit(u)
            if folds(UNITS - 1):
                sum_folded(UNITS - 1)

            for c in range(1, CH, 2):
                dve.wait_ge(hT_in_psum, c + 1)
                nc.vector.tensor_copy(hT[0:chunk_rows[c], c, :], psum[0:chunk_rows[c], c % TILES, :, :].rearrange("p a b -> p (a b)")
                                      ).then_inc(hT_ready[1], 1)

        @block.tensor
        def _(pe):
            def transpose_x(j):
                pe.wait_ge(gathered[j % GROUP], 16 * BT * (j // GROUP + 1))
                if j > 1:
                    if host(j - 1) > 0:
                        pe.wait_ge(mult_done, TILES * host(j - 1))
                    pe.wait_ge(xT_low_ready, j - 1)
                for t in range(BT):
                    last = nc.tensor.transpose(psum[:, TILES - 1, t // 4, (t % 4) * PART:(t % 4 + 1) * PART],
                                               x[:, t, j, :], ident[:, :])
                last.then_inc(xT_in_psum, 1)

            def field(j):
                par = j % 2

                def unit(u, i0, pairs):
                    cols = pairs * EMBED
                    part = held(pe, split_slot(u) + COLS - cols)
                    high, low = k_high[:, bass.ds(part, cols)], k_low[:, bass.ds(part, cols)]
                    pe.wait_ge(k_low_ready, u + 1)
                    for t in range(TILES):
                        if t == XT_AT and isinstance(u, int) and u == host(j) and j + 1 < FIELDS:
                            transpose_x(j + 1)
                        if not (isinstance(u, int) and u == 0):
                            pe.wait_ge(mult_done, TILES * (u - 1) + t + 1)
                        if t == TILES - 1 and j + 1 < FIELDS and isinstance(u, int) and u == host(j):
                            pe.wait_ge(xT_low_ready, j + 1)
                        for b in range(2):
                            out = psum[:, t, b, 0:cols]
                            bt = 2 * t + b
                            x_high = xT[:, par, 0, bt * PART:(bt + 1) * PART]
                            x_low = xT[:, par, 1, bt * PART:(bt + 1) * PART]
                            nc.tensor.matmul(out, x_high, high, start=True, stop=False)
                            nc.tensor.matmul(out, x_high, low, start=False, stop=False)
                            last = nc.tensor.matmul(out, x_low, high, start=False, stop=True)
                        last.then_inc(dots_ready, 1)

                pe.wait_ge(xT_low_ready, j)
                units(pe, j, unit)

            pe.wait_ge(ident_ready, 2)
            transpose_x(1)
            for j in range(1, FIELDS):
                field(j)

            pe.wait_ge(h_loaded, 32)
            pe.wait_ge(mult_done, UNITS * TILES)
            for c in range(CH):
                if c >= TILES:
                    pe.wait_ge(hT_ready[c % 2], (c - TILES) // 2 + 1)
                for t in range(BT):
                    last = nc.tensor.transpose(psum[0:chunk_rows[c], c % TILES, t // 4, (t % 4) * PART:(t % 4 + 1) * PART],
                                               h[:, t, c * PART:c * PART + chunk_rows[c]], ident[:, :])
                last.then_inc(hT_in_psum, 1)
            pe.wait_ge(w1_loaded, 32)
            pe.wait_ge(hT_ready[0], -(-CH // 2))
            pe.wait_ge(hT_ready[1], CH // 2)
            for c in range(C1):
                for half in range(2):
                    for k in range(CH):
                        rows = chunk_rows[k]
                        last = nc.tensor.matmul(psum[:, c, half, :], w1[0:rows, k, c * PART:(c + 1) * PART],
                                                hT[0:rows, k, half * HALF:(half + 1) * HALF], start=k == 0, stop=k == CH - 1)
                    last.then_inc(l1_in_psum, 1)
            pe.wait_ge(w_loaded, 64)
            pe.wait_ge(l1_ready, 2 * C1)
            for c in range(C2):
                for half in range(2):
                    for k in range(C1):
                        last = nc.tensor.matmul(psum[:, c, half, :], w2[:, k, c * PART:(c + 1) * PART],
                                                l1T[:, k, half * HALF:(half + 1) * HALF], start=k == 0, stop=k == C1 - 1)
                    last.then_inc(l2_in_psum, 1)
            pe.wait_ge(l2_ready, 2 * C2)
            for half in range(2):
                for k in range(C2):
                    last = nc.tensor.matmul(psum[0:1, C2, half, :], w3[:, k:k + 1],
                                            l2T[:, k, half * HALF:(half + 1) * HALF], start=k == 0, stop=k == C2 - 1)
                last.then_inc(y_in_psum, 1)


def kernel(**inputs):
    import concourse.bacc as bacc
    from concourse.bass_utils import run_bass_kernel_spmd

    number = {}
    for i in range(FIELDS - 1):
        for j in range(i + 1, FIELDS):
            number[i, j] = len(number)
    order = [number[i, j] for j in range(1, FIELDS) for i in range(j)]

    nc = bacc.Bacc("TRN2", target_bir_lowering=False, num_devices=1, dynamic_dma_scratch_size=SCRATCH)
    arrays, aps = {}, {}

    def give(name, a):
        a = np.ascontiguousarray(a)
        arrays[name] = a
        aps[name] = nc.dram_tensor(name, a.shape, mybir.dt.from_np(a.dtype), kind="ExternalInput").ap()
        return aps[name]

    dense_ctx = give("dense_ctx", inputs["dense_ctx"])
    ids = give("ids", inputs["ids"])
    tables = [give(f"tbl_{f}", inputs[f"tbl_{f}"]) for f in range(FIELDS)]
    kernels = give("kernels", np.asarray(inputs["L0_rec_kernel"])[:, order, :].reshape(EMBED, PAIRS * EMBED))
    w1 = np.asarray(inputs["W_top1"])
    W1 = give("W1", np.concatenate([w1[order], w1[PAIRS:]]))
    b1 = give("b1", inputs["b_top1"])
    W2 = give("W2", inputs["W_top2"])
    b2 = give("b2", inputs["b_top2"])
    W3 = give("W3", inputs["W_top3"])
    y = nc.dram_tensor("y", (BATCH, 1), F32, kind="ExternalOutput").ap()
    z_dram = nc.dram_tensor("z_dram", (BATCH, PAIRS), F32, kind="Internal").ap()
    tower(nc, dense_ctx, ids, tables, kernels, W1, b1, W2, b2, W3, y, z_dram)
    result = run_bass_kernel_spmd(nc, [arrays], core_ids=[0])
    return result.results[0]["y"]
```

```python
from contextlib import ExitStack
from functools import cache

import numpy as np

import concourse.bass as bass
from concourse import mybir

F32 = mybir.dt.float32
F32R = mybir.dt.float32r
I32 = mybir.dt.int32
U32 = mybir.dt.uint32
ALU = mybir.AluOpType
ACT = mybir.ActivationFunctionType
AX = mybir.AxisListType

PART = 128
FIELDS = 40
EMBED = 128
BATCH = 1024
DENSE = 16
PAIRS = FIELDS * (FIELDS - 1) // 2
IN1, OUT1, OUT2 = PAIRS + DENSE, 512, 256
LAST = FIELDS - 1
EARLY = PAIRS - LAST
BT = BATCH // PART
GROUP = 4
COLS = GROUP * EMBED
TILES = BT // 2
RAW, SPLIT = 3, 3
ZS = 3
AHEAD = 2
FOLDS = 4
SCRATCH = 8192

FIRST_GATHERED = 9
LEAD = 2.6
POOL_FROM = 6
FOLD_FROM = 12
LATE_UNTIL = 8

KL_AT = 3
SUM_AT = 2
XT_AT = 2
W1_EARLY = 2


def row_start(j):
    return j * (j - 1) // 2


def heads(j):
    short = {0: [], 1: [3, 2] if j > 1 else [1], 2: [2], 3: [3]}[j % GROUP]
    return short + [GROUP] * ((j - sum(short)) // GROUP if j < LATE_UNTIL else 1)


def host(j):
    return first_unit(j) + len(heads(j)) - 1


def looped(j):
    return (j - sum(heads(j))) // GROUP


@cache
def first_unit(j):
    return sum(len(heads(f)) + looped(f) for f in range(1, j))


@cache
def unit_field(u):
    return next(f for f in range(1, FIELDS) if first_unit(f + 1) > u)


@cache
def unit_pairs(u):
    j = unit_field(u)
    return (heads(j) + [GROUP] * looped(j))[u - first_unit(j)]


def unit_partner(u):
    return sum(unit_pairs(v) for v in range(first_unit(unit_field(u)), u))


UNITS = first_unit(FIELDS)
POOL_FIRST = first_unit(POOL_FROM) + AHEAD


def reducer(u, t):
    if t % 2:
        return "act"
    return "pool" if t == 0 and folds(u) else "dve"


def folds(u):
    return unit_field(u) >= FOLD_FROM and unit_pairs(u) == GROUP


def gathers_through(u):
    j = unit_field(u)
    at = j + (u + 1 - first_unit(j)) / (first_unit(j + 1) - first_unit(j))
    return max(BT * FIRST_GATHERED, int(BT * min(FIELDS, at + LEAD)))


@cache
def folded_before(u):
    return sum(folds(v) for v in range(u))


def fold_slot(u):
    return folded_before(u) % 2 * 2


def tower(nc, dense_ctx, ids, tables, kernels, W1, b1, W2, b2, W3, y, z_dram):
    ctx = ExitStack()
    with ctx:
        def sb(name, shape, dt=F32):
            return ctx.enter_context(nc.sbuf_tensor(name, shape, dt))

        def sem(name):
            return ctx.enter_context(nc.semaphore(name))

        with nc.sbuf_tensor("x", [PART, BT, FIELDS, EMBED], F32) as x:
            pass
        x_parts = [sb(f"x_parts{t}", [PART, FIELDS, EMBED], F32R) for t in range(BT)]
        xT = sb("xT", [PART, 2, 2, BATCH], F32R)
        k_raw = sb("k_raw", [PART, RAW * COLS])
        k_high = sb("k_high", [PART, SPLIT * COLS], F32R)
        k_low = sb("k_low", [PART, SPLIT * COLS], F32R)
        prod = sb("prod", [PART, TILES, 2, COLS])
        z = sb("z", [PART, ZS, BT, FIELDS])
        idx = sb("idx", [PART, BT, FIELDS], I32)
        ident = sb("ident", [PART, PART])
        psum = ctx.enter_context(nc.psum_tensor("psum", [PART, TILES, 2, COLS], F32))

        ids_loaded = sem("ids_loaded")
        gathered = [sem(f"gathered{r}") for r in range(GROUP)]
        ident_ready = sem("ident_ready")
        k_loaded = sem("k_loaded")
        k_high_ready = sem("k_high_ready")
        k_low_ready = sem("k_low_ready")
        xT_in_psum = sem("xT_in_psum")
        xT_high_ready = sem("xT_high_ready")
        xT_low_ready = sem("xT_low_ready")
        dots_ready = sem("dots_ready")
        mult_done = sem("mult_done")
        folded = sem("folded")
        summed = {t: sem(f"act_summed{t}") for t in range(1, TILES, 2)}
        fold_summed = sem("fold_summed")
        z_stored = [sem(f"z_stored{s}") for s in range(ZS)]
        h_loaded = sem("h_loaded")
        w1_loaded = sem("w1_loaded")
        w_loaded = sem("w_loaded")
        w1_high_ready = sem("w1_high_ready")
        w1_low_ready = sem("w1_low_ready")
        hT_in_psum = sem("hT_in_psum")
        hT_high_ready = sem("hT_high_ready")
        hT_low_ready = sem("hT_low_ready")
        l1_in_psum = sem("l1_in_psum")
        l1_ready = [sem(f"l1_ready{e}") for e in ("_act", "_dve")]
        l2_in_psum = sem("l2_in_psum")
        l2_ready = [sem(f"l2_ready{e}") for e in ("_act", "_dve")]
        y_in_psum = sem("y_in_psum")
        y_ready = sem("y_ready")
        y_stored = sem("y_stored")


        chunk_rows = [min(PART, EARLY + DENSE - at) for at in range(0, EARLY + DENSE, PART)] + [LAST]
        CH, C1, C2 = len(chunk_rows), OUT1 // PART, OUT2 // PART
        HALF = BATCH // 2

        def in_x(f, t, n, parts=False):
            tile = x_parts[t][:, :, :] if parts else x[:, t, :, :]
            return tile[:, f:f - (-n // EMBED), :].rearrange("p f d -> p (f d)")[:, 0:n]

        def free_from(f):
            return TILES * (1 + next(u for u in range(first_unit(LAST), UNITS) if unit_partner(u) + unit_pairs(u) >= f))

        W1_AT, H_AT = 0, OUT1 // EMBED
        W1_HIGH_AT = H_AT + (CH - 1) * PART // EMBED
        W1_LOW_AT = W1_HIGH_AT + OUT1 // EMBED
        HT_HIGH_AT = W1_LOW_AT + OUT1 // EMBED
        HT_LOW_AT = HT_HIGH_AT + BATCH // EMBED
        w1 = [in_x(W1_AT, c, OUT1) for c in range(CH)]
        w1_high = [in_x(W1_HIGH_AT, c, OUT1, parts=True) for c in range(CH)]
        w1_low = [in_x(W1_LOW_AT, c, OUT1, parts=True) for c in range(CH)]
        h = x[:, :, H_AT:H_AT + CH - 1, :].rearrange("p t f d -> p t (f d)")
        hT_high = [in_x(HT_HIGH_AT, c, BATCH, parts=True) for c in range(CH)]
        hT_low = [in_x(HT_LOW_AT, c, BATCH, parts=True) for c in range(CH)]
        w2 = in_x(HT_HIGH_AT, BT - 1, C1 * OUT2).rearrange("p (c n) -> p c n", c=C1)
        vectors = in_x(W1_AT, BT - 1, C2 + C1 + C2)
        w3, bias1, bias2 = vectors[:, 0:C2], vectors[:, C2:C2 + C1], vectors[:, C2 + C1:]
        hT_psum = [psum[0:rows, TILES - 1 if c else 0, :, :].rearrange("p a b -> p (a b)")
                   for c, rows in enumerate(chunk_rows)]
        l1T = [in_x(0, c, BATCH) for c in range(C1)]
        l2T = [in_x(0, C1 + c, BATCH) for c in range(C2)]
        y_row = in_x(0, C1 + C2, BATCH)

        def units(eng, j, body, peel=0):
            u, i0 = first_unit(j), 0
            for pairs in heads(j):
                body(u, i0, pairs)
                u, i0 = u + 1, i0 + pairs
            if looped(j) > peel:
                with eng.Fori(0, looped(j) - peel) as g:
                    body(u + g, i0 + g * GROUP, GROUP)
            for g in range(looped(j) - peel, looped(j) if peel else 0):
                body(u + g, i0 + g * GROUP, GROUP)

        def held(eng, value):
            return value if isinstance(value, int) else eng.compute_val(value)

        def raw_slot(u):
            return (u % RAW) * COLS

        def split_slot(u):
            return (u % SPLIT) * COLS

        block = ctx.enter_context(nc.Block())

        @block.sync
        def _(sp):
            sp.dma_start(idx[:, :, :], ids.rearrange("(t p) f -> p t f", p=PART)).then_inc(ids_loaded, 16)

            def load(u, i0, pairs, j):
                cols = pairs * EMBED if j < GROUP else COLS
                pair0 = row_start(j) + i0 + pairs - cols // EMBED
                to, source = held(sp, raw_slot(u) + COLS - cols), held(sp, pair0 * EMBED)
                earlier, freed = held(sp, u * 16), held(sp, u - RAW + 1)
                if j > 1:
                    sp.wait_ge(k_loaded, earlier)
                if j >= GROUP:
                    sp.wait_ge(k_low_ready, freed)
                sp.dma_start(k_raw[:, bass.ds(to, cols)], kernels[:, bass.ds(source, cols)]).then_inc(k_loaded, 16)

            def load_w1(chunks):
                for c in chunks:
                    row, rows = sum(chunk_rows[:c]), chunk_rows[c]
                    sp.dma_start(w1[c][0:rows, :], W1[row:row + rows, :]).then_inc(w1_loaded, 16)

            def load_z(tiles):
                rows = slice(tiles[0] * PART, (tiles[-1] + 1) * PART)
                sp.dma_start(h[:, tiles[0]:tiles[-1] + 1, 0:EARLY],
                             z_dram[rows, :].rearrange("(t p) n -> p t n", p=PART)).then_inc(h_loaded, 16)

            def load_last(u, i0, pairs):
                load(u, i0, pairs, LAST)
                if not isinstance(u, int):
                    return
                if u == UNITS - 6:
                    sp.wait_ge(mult_done, free_from(H_AT))
                    load_w1(range(0, 3))
                elif u == UNITS - 5:
                    load_w1(range(3, CH))
                elif u == UNITS - 4:
                    sp.wait_ge(mult_done, free_from(W1_HIGH_AT))
                    for s in range(ZS):
                        sp.wait_ge(z_stored[s], 16 * len(range(s or ZS, LAST, ZS)))
                    load_z(range(0, 3))
                elif u == UNITS - 3:
                    load_z(range(3, 6))
                elif u == UNITS - 2:
                    load_z(range(6, BT))
                    sp.dma_start(h[:, :, EARLY:EARLY + DENSE],
                                 dense_ctx.rearrange("(t p) n -> p t n", p=PART)).then_inc(h_loaded, 16)

            for j in range(1, LAST):
                units(sp, j, lambda u, i0, pairs: load(u, i0, pairs, j))
            units(sp, LAST, load_last, peel=6)
            with nc.allow_non_contiguous_dma(reason="vectors of at most 512 elements, one per partition"):
                sp.dma_start(w3, W3.rearrange("(c p) n -> p (c n)", p=PART)).then_inc(w_loaded, 16)
                sp.dma_start(bias1, b1.rearrange("(c p) -> p c", p=PART)).then_inc(w_loaded, 16)
                sp.dma_start(bias2, b2.rearrange("(c p) -> p c", p=PART)).then_inc(w_loaded, 16)
            sp.wait_ge(mult_done, free_from(HT_LOW_AT))
            sp.dma_start(w2, W2.rearrange("(c p) n -> p c n", p=PART)).then_inc(w_loaded, 16)
            sp.wait_ge(y_ready, 2)
            sp.dma_start(y.rearrange("b n -> n b"), y_row[0:1, :]).then_inc(y_stored, 16)
            sp.wait_ge(y_stored, 16)

        @block.gpsimd
        def _(pool):
            nc.gpsimd.memset(ident[:, :], 0.0).then_inc(ident_ready, 1)
            pool.wait_ge(ident_ready, 1)
            nc.gpsimd.affine_select(out=ident[:, :], in_=ident[:, :], compare_op=ALU.not_equal, fill=1.0,
                                    base=0, pattern=[[-1, PART]], channel_multiplier=1).then_inc(ident_ready, 1)
            pool.wait_ge(ids_loaded, 16)

            def gather(n):
                f, t = divmod(n, BT)
                if f >= GROUP and t == 0:
                    pool.wait_ge(gathered[f % GROUP], 16 * BT * (f // GROUP))
                nc.gpsimd.indirect_dma_start(
                    x[:, t, f, :], None, tables[f],
                    bass.IndirectOffsetOnAxis(ap=idx[:, t, f:f + 1].bitcast(U32), axis=0)
                ).then_inc(gathered[f % GROUP], 16)

            def split_low(u):
                cols = unit_pairs(u) * EMBED
                raw_end, end = raw_slot(u) + COLS, split_slot(u) + COLS
                pool.wait_ge(k_high_ready, u + 1)
                pool.wait_ge(dots_ready, TILES * (u - SPLIT + 1))
                if u == POOL_FIRST:
                    pool.wait_ge(k_low_ready, u)
                nc.gpsimd.tensor_tensor(k_low[:, end - cols:end], k_raw[:, raw_end - cols:raw_end],
                                        k_high[:, end - cols:end].bitcast(F32), ALU.subtract).then_inc(k_low_ready, 1)

            def fold(u):
                pool.wait_ge(mult_done, TILES * u + 1)
                p = prod[:, fold_slot(u), :, :].rearrange("p b (n d) -> p b n d", d=EMBED)
                for s in range(FOLDS):
                    w = EMBED >> (s + 1)
                    if s:
                        pool.wait_ge(folded, FOLDS * folded_before(u) + s)
                    nc.gpsimd.tensor_tensor(p[:, :, :, 0:w], p[:, :, :, 0:w], p[:, :, :, w:2 * w],
                                            ALU.add).then_inc(folded, 1)

            for f in (1, 0, *range(2, FIRST_GATHERED)):
                for t in range(BT):
                    gather(f * BT + t)
            done = FIRST_GATHERED * BT
            def split_w1(c):
                rows = chunk_rows[c]
                if c == 0:
                    pool.wait_ge(w1_loaded, 16 * CH)
                    pool.wait_ge(mult_done, free_from(HT_HIGH_AT))
                nc.gpsimd.tensor_copy(w1_high[c][0:rows, :], w1[c][0:rows, :]).then_inc(w1_high_ready, 1)
                pool.wait_ge(w1_high_ready, c + 1)
                nc.gpsimd.tensor_tensor(w1_low[c][0:rows, :], w1[c][0:rows, :], w1_high[c][0:rows, :].bitcast(F32),
                                        ALU.subtract).then_inc(w1_low_ready, 1)

            for u in range(UNITS):
                j = unit_field(u)
                if folds(u):
                    fold(u)
                if POOL_FIRST <= u + AHEAD < UNITS:
                    split_low(u + AHEAD)
                for n in range(done, gathers_through(u)):
                    gather(n)
                done = gathers_through(u)
                if u >= UNITS - W1_EARLY:
                    split_w1(u - (UNITS - W1_EARLY))
            for c in range(W1_EARLY, CH):
                split_w1(c)

        @block.scalar
        def _(act):
            def split_high(u, pairs=GROUP):
                skip = COLS - pairs * EMBED
                raw, part = held(act, raw_slot(u) + skip), held(act, split_slot(u) + skip)
                act.wait_ge(k_loaded, 16 * (u + 1))
                if not isinstance(u, int) or u >= SPLIT:
                    act.wait_ge(dots_ready, TILES * (u - SPLIT + 1))
                    act.wait_ge(k_low_ready, u - SPLIT + 1)
                nc.scalar.activation(k_high[:, bass.ds(part, COLS - skip)], k_raw[:, bass.ds(raw, COLS - skip)],
                                     ACT.Copy).then_inc(k_high_ready, 1)

            def split_x_high(j):
                for half in range(2):
                    act.wait_ge(xT_in_psum, 2 * (j - 1) + half + 1)
                    nc.scalar.activation(xT[:, j % 2, 0, half * HALF:(half + 1) * HALF], psum[:, TILES - 1, half, :],
                                         ACT.Copy).then_inc(xT_high_ready, 1)

            def store(j):
                for t in summed:
                    act.wait_ge(summed[t], first_unit(j + 1))
                act.wait_ge(mult_done, TILES * first_unit(j + 1))
                if folded_before(first_unit(j + 1)):
                    act.wait_ge(fold_summed, folded_before(first_unit(j + 1)))
                zj = z_dram[:, row_start(j):row_start(j) + j].rearrange("(t p) n -> p t n", p=PART)
                with nc.allow_non_contiguous_dma(reason="field 1 has one pair"):
                    act.dma_start(zj, z[:, j % ZS, :, 0:j]).then_inc(z_stored[j % ZS], 16)

            def sum_tile(u, t, j, i0, pairs, between=None):
                act.wait_ge(mult_done, TILES * u + t + 1)
                for b in range(2):
                    if b and between:
                        between()
                    for n in range(pairs):
                        p = prod[:, t, b, n * EMBED:(n + 1) * EMBED]
                        last = nc.scalar.activation(p, p, ACT.Copy, accum_out=z[:, j % ZS, 2 * t + b, bass.ds(i0 + n, 1)])
                last.then_inc(summed[t], 1)

            def field(j):
                def unit(u, i0, pairs):
                    makes_x = isinstance(u, int) and u == host(j) and j + 1 < FIELDS
                    if isinstance(u, int) and u > 0:
                        before = unit_field(u - 1), unit_partner(u - 1), unit_pairs(u - 1)
                    else:
                        before = j, i0 - GROUP, GROUP
                    if isinstance(u, int) and u == 0:
                        split_x_high(2)
                    else:
                        sum_tile(u - 1, TILES - 1, *before, (lambda: split_x_high(j + 1)) if makes_x else None)
                    if not isinstance(u, int):
                        split_high(u + AHEAD)
                    elif u + AHEAD < UNITS:
                        split_high(u + AHEAD, unit_pairs(u + AHEAD) if u + AHEAD < RAW else GROUP)
                    sum_tile(u, 1, j, i0, pairs)
                    if isinstance(u, int) and u == host(j) and j > 1:
                        store(j - 1)

                if j > ZS:
                    act.wait_ge(z_stored[j % ZS], 16 * ((j - 1) // ZS))
                if j < FIELDS - 1:
                    units(act, j, unit)
                else:
                    units(act, j, unit, peel=AHEAD)

            for u in range(AHEAD):
                split_high(u, unit_pairs(u))
            split_x_high(1)
            for j in range(1, FIELDS):
                field(j)

            def split_h_high(c):
                act.wait_ge(hT_in_psum, c + 1)
                nc.scalar.activation(hT_high[c][0:chunk_rows[c], :], hT_psum[c], ACT.Copy).then_inc(hT_high_ready, 1)

            act.wait_ge(mult_done, free_from(HT_LOW_AT))
            split_h_high(0)
            sum_tile(UNITS - 1, TILES - 1, LAST, unit_partner(UNITS - 1), unit_pairs(UNITS - 1))
            for c in range(1, CH):
                split_h_high(c)
            act.wait_ge(w_loaded, 64)
            for c in range(C1):
                act.wait_ge(l1_in_psum, 2 * c + 1)
                nc.scalar.activation(l1T[c][:, 0:HALF], psum[:, c, 0, :], ACT.Relu,
                                     bias=bias1[:, c:c + 1]).then_inc(l1_ready[0], 1)
            for c in range(C2):
                act.wait_ge(l2_in_psum, 2 * c + 1)
                nc.scalar.activation(l2T[c][:, 0:HALF], psum[:, c, 0, :], ACT.Relu,
                                     bias=bias2[:, c:c + 1]).then_inc(l2_ready[0], 1)
            for half in range(2):
                act.wait_ge(y_in_psum, half + 1)
                nc.scalar.activation(y_row[0:1, half * HALF:(half + 1) * HALF], psum[0:1, C2, half, :],
                                     ACT.Copy).then_inc(y_ready, 1)

        @block.vector
        def _(dve):
            def split_low(u):
                cols = unit_pairs(u) * EMBED
                raw_end, end = raw_slot(u) + COLS, split_slot(u) + COLS
                dve.wait_ge(k_high_ready, u + 1)
                if u >= SPLIT:
                    dve.wait_ge(dots_ready, TILES * (u - SPLIT + 1))
                nc.vector.tensor_tensor(k_low[:, end - cols:end], k_raw[:, raw_end - cols:raw_end],
                                        k_high[:, end - cols:end].bitcast(F32), ALU.subtract).then_inc(k_low_ready, 1)

            def split_x_low(j):
                for half in range(2):
                    bs = slice(half * HALF, (half + 1) * HALF)
                    dve.wait_ge(xT_high_ready, 2 * (j - 1) + half + 1)
                    nc.vector.tensor_tensor(xT[:, j % 2, 1, bs], psum[:, TILES - 1, half, :],
                                            xT[:, j % 2, 0, bs].bitcast(F32), ALU.subtract).then_inc(xT_low_ready, 1)

            def sum_folded(u):
                j, i0, pairs = unit_field(u), unit_partner(u), unit_pairs(u)
                dve.wait_ge(folded, FOLDS * (folded_before(u) + 1))
                p = prod[:, fold_slot(u), :, :].rearrange("p b (n d) -> p b n d", d=EMBED)
                nc.vector.tensor_reduce(z[:, j % ZS, 0:2, i0:i0 + pairs], p[:, :, :, 0:EMBED >> FOLDS],
                                        AX.X, ALU.add).then_inc(fold_summed, 1)

            def unit(u):
                j, i0, pairs = unit_field(u), unit_partner(u), unit_pairs(u)
                cols = pairs * EMBED
                for t in range(TILES):
                    if t == KL_AT and u + AHEAD < POOL_FIRST:
                        split_low(u + AHEAD)
                    if t == XT_AT and u == host(j) and j + 1 < FIELDS:
                        split_x_low(j + 1)
                    if t == SUM_AT and u and folds(u - 1):
                        sum_folded(u - 1)
                    dve.wait_ge(dots_ready, TILES * u + t + 1)
                    if reducer(u, t) == "dve":
                        for b in range(2):
                            for n in range(pairs):
                                p = psum[:, t, b, n * EMBED:(n + 1) * EMBED]
                                last = nc.vector.scalar_tensor_tensor(
                                    p, p, 1.0, x[:, 2 * t + b, i0 + n, :], ALU.mult, ALU.mult,
                                    accum_out=z[:, j % ZS, 2 * t + b, i0 + n:i0 + n + 1])
                        last.then_inc(mult_done, 1)
                        continue
                    if reducer(u, t) == "pool":
                        slot = fold_slot(u)
                        if folded_before(u) >= 2:
                            dve.wait_ge(fold_summed, folded_before(u) - 1)
                    else:
                        slot = t
                        if u:
                            dve.wait_ge(summed[t], u)
                    nc.vector.tensor_tensor(
                        prod[:, slot, :, 0:cols], psum[:, t, :, 0:cols],
                        x[:, 2 * t:2 * t + 2, i0:i0 + pairs, :].rearrange("p b n d -> p b (n d)"),
                        ALU.mult).then_inc(mult_done, 1)

            for u in range(AHEAD):
                split_low(u)
            split_x_low(1)
            dve.wait_ge(gathered[0], 16 * BT)
            for j in range(1, FIELDS):
                if j > ZS:
                    dve.wait_ge(z_stored[j % ZS], 16 * ((j - 1) // ZS))
                for u in range(first_unit(j), first_unit(j + 1)):
                    unit(u)
            for c in range(CH):
                rows = chunk_rows[c]
                dve.wait_ge(hT_high_ready, c + 1)
                nc.vector.tensor_tensor(hT_low[c][0:rows, :], hT_psum[c], hT_high[c][0:rows, :].bitcast(F32),
                                        ALU.subtract).then_inc(hT_low_ready, 1)
                if c == 0 and folds(UNITS - 1):
                    sum_folded(UNITS - 1)
            dve.wait_ge(w_loaded, 64)
            for c in range(C1):
                dve.wait_ge(l1_in_psum, 2 * c + 2)
                nc.vector.tensor_scalar(l1T[c][:, HALF:BATCH], psum[:, c, 1, :], bias1[:, c:c + 1], 0.0,
                                        ALU.add, ALU.max).then_inc(l1_ready[1], 1)
            for c in range(C2):
                dve.wait_ge(l2_in_psum, 2 * c + 2)
                nc.vector.tensor_scalar(l2T[c][:, HALF:BATCH], psum[:, c, 1, :], bias2[:, c:c + 1], 0.0,
                                        ALU.add, ALU.max).then_inc(l2_ready[1], 1)

        @block.tensor
        def _(pe):
            def transpose_x(j):
                pe.wait_ge(gathered[j % GROUP], 16 * BT * (j // GROUP + 1))
                if j > 1:
                    pe.wait_ge(xT_low_ready, 2 * (j - 1))
                    if host(j - 1) > 0:
                        pe.wait_ge(mult_done, TILES * host(j - 1))
                for t in range(BT):
                    last = nc.tensor.transpose(psum[:, TILES - 1, t // 4, (t % 4) * PART:(t % 4 + 1) * PART],
                                               x[:, t, j, :], ident[:, :])
                    if t % 4 == 3:
                        last.then_inc(xT_in_psum, 1)

            def field(j):
                par = j % 2

                def unit(u, i0, pairs):
                    cols = pairs * EMBED
                    part = held(pe, split_slot(u) + COLS - cols)
                    high, low = k_high[:, bass.ds(part, cols)], k_low[:, bass.ds(part, cols)]
                    pe.wait_ge(k_low_ready, u + 1)
                    for t in range(TILES):
                        if t == XT_AT and isinstance(u, int) and u == host(j) and j + 1 < FIELDS:
                            transpose_x(j + 1)
                        if not (isinstance(u, int) and u == 0):
                            pe.wait_ge(mult_done, TILES * (u - 1) + t + 1)
                        if t == TILES - 1 and j + 1 < FIELDS and isinstance(u, int) and u == host(j):
                            pe.wait_ge(xT_low_ready, 2 * (j + 1))
                        for b in range(2):
                            out = psum[:, t, b, 0:cols]
                            bt = 2 * t + b
                            x_high = xT[:, par, 0, bt * PART:(bt + 1) * PART]
                            x_low = xT[:, par, 1, bt * PART:(bt + 1) * PART]
                            nc.tensor.matmul(out, x_high, high, start=True, stop=False)
                            nc.tensor.matmul(out, x_high, low, start=False, stop=False)
                            last = nc.tensor.matmul(out, x_low, high, start=False, stop=True)
                        last.then_inc(dots_ready, 1)

                pe.wait_ge(xT_low_ready, 2 * j)
                units(pe, j, unit)

            pe.wait_ge(ident_ready, 2)
            transpose_x(1)
            for j in range(1, FIELDS):
                field(j)

            def transpose_h(c):
                rows = chunk_rows[c]
                if c == 0:
                    pe.wait_ge(mult_done, TILES * (UNITS - 1) + 1)
                elif c == 1:
                    pe.wait_ge(mult_done, TILES * UNITS)
                else:
                    pe.wait_ge(hT_low_ready, c)
                if c == CH - 1:
                    for t in summed:
                        pe.wait_ge(summed[t], UNITS)
                    pe.wait_ge(fold_summed, folded_before(UNITS))
                for t in range(BT):
                    source = z[:, LAST % ZS, t, 0:LAST] if c == CH - 1 else h[:, t, c * PART:c * PART + rows]
                    last = nc.tensor.transpose(hT_psum[c][:, t * PART:(t + 1) * PART], source, ident[:, :])
                last.then_inc(hT_in_psum, 1)

            def layer1(k, c):
                rows, outs = chunk_rows[k], slice(c * PART, (c + 1) * PART)
                w_high, w_low = w1_high[k][0:rows, outs], w1_low[k][0:rows, outs]
                for w, i, first, final in ((w_high, hT_high, True, False), (w_high, hT_low, False, False),
                                           (w_low, hT_high, False, True)):
                    for half in range(2):
                        last = nc.tensor.matmul(psum[:, c, half, :], w, i[k][0:rows, half * HALF:(half + 1) * HALF],
                                                start=first and k == 0, stop=final and k == CH - 1)
                        if final and k == CH - 1:
                            last.then_inc(l1_in_psum, 1)

            pe.wait_ge(h_loaded, 16 * 4)
            transpose_h(0)
            for k in range(CH):
                pe.wait_ge(hT_low_ready, k + 1)
                pe.wait_ge(w1_low_ready, k + 1)
                if k + 1 < CH:
                    transpose_h(k + 1)
                for c in range(C1 - 1):
                    layer1(k, c)
            for k in range(CH):
                layer1(k, C1 - 1)
            pe.wait_ge(w_loaded, 64)
            for k in range(C1):
                for e in range(2):
                    pe.wait_ge(l1_ready[e], max(k + 1, C2))
                for c in range(C2):
                    for half in range(2):
                        last = nc.tensor.matmul(psum[:, c, half, :], w2[:, k, c * PART:(c + 1) * PART],
                                                l1T[k][:, half * HALF:(half + 1) * HALF], start=k == 0, stop=k == C1 - 1)
                        if k == C1 - 1:
                            last.then_inc(l2_in_psum, 1)
            for half in range(2):
                pe.wait_ge(l2_ready[half], C2)
                for k in range(C2):
                    last = nc.tensor.matmul(psum[0:1, C2, half, :], w3[:, k:k + 1],
                                            l2T[k][:, half * HALF:(half + 1) * HALF], start=k == 0, stop=k == C2 - 1)
                last.then_inc(y_in_psum, 1)


def kernel(**inputs):
    import concourse.bacc as bacc
    from concourse.bass_utils import run_bass_kernel_spmd

    number = {}
    for i in range(FIELDS - 1):
        for j in range(i + 1, FIELDS):
            number[i, j] = len(number)
    order = [number[i, j] for j in range(1, FIELDS) for i in range(j)]

    nc = bacc.Bacc("TRN2", target_bir_lowering=False, num_devices=1, dynamic_dma_scratch_size=SCRATCH)
    arrays, aps = {}, {}

    def give(name, a):
        a = np.ascontiguousarray(a)
        arrays[name] = a
        aps[name] = nc.dram_tensor(name, a.shape, mybir.dt.from_np(a.dtype), kind="ExternalInput").ap()
        return aps[name]

    dense_ctx = give("dense_ctx", inputs["dense_ctx"])
    ids = give("ids", inputs["ids"])
    tables = [give(f"tbl_{f}", inputs[f"tbl_{f}"]) for f in range(FIELDS)]
    kernels = give("kernels", np.asarray(inputs["L0_rec_kernel"])[:, order, :].reshape(EMBED, PAIRS * EMBED))
    w1 = np.asarray(inputs["W_top1"])
    W1 = give("W1", np.concatenate([w1[order[:EARLY]], w1[PAIRS:], w1[order[EARLY:]]]))
    b1 = give("b1", inputs["b_top1"])
    W2 = give("W2", inputs["W_top2"])
    b2 = give("b2", inputs["b_top2"])
    W3 = give("W3", inputs["W_top3"])
    y = nc.dram_tensor("y", (BATCH, 1), F32, kind="ExternalOutput").ap()
    z_dram = nc.dram_tensor("z_dram", (BATCH, EARLY), F32, kind="Internal").ap()
    tower(nc, dense_ctx, ids, tables, kernels, W1, b1, W2, b2, W3, y, z_dram)
    result = run_bass_kernel_spmd(nc, [arrays], core_ids=[0])
    return result.results[0]["y"]
```
